# Optimizing a Trainium2 kernel written in Bass

```python
import numpy as np
import jax
import jax.numpy as jnp

def _softmax(x, axis=-1):
    return jax.nn.softmax(x, axis=axis)

def _gelu(x):
    return jax.nn.gelu(x, approximate=True)

def _silu(x):
    return jax.nn.silu(x)

def _sigmoid(x):
    return jax.nn.sigmoid(x)

def _layernorm(x, axis=-1, eps=1e-05):
    m = jnp.mean(x, axis=axis, keepdims=True)
    v = jnp.var(x, axis=axis, keepdims=True)
    return (x - m) / jnp.sqrt(v + eps)

def _scatter_add(tgt, idx, src, axis=0):
    return tgt.at[idx].add(src)

def _segment_sum(src, seg, n):
    return jax.ops.segment_sum(src, seg, n)
kernel_name = 'mk_rec_standalone_d1_rec_r8_3d0e9f'

def setup_inputs(seed: int=0):
    np.random.seed(seed)
    _w = jnp.asarray

    def _rec_inputs():
        import jax
        import jax.numpy as jnp
        _rk = jax.random.key(seed)
        r_inputs = -0.000520686 + 1.00062 * jax.random.normal(jax.random.fold_in(_rk, 1), (512, 256), jnp.float32)
        return r_inputs
    r_inputs = _rec_inputs()

    def _L0_rec_setup():
        import jax, jax.numpy as jnp
        import numpy as np
        NUM_FIELDS = 32
        EMBED_DIM = 64
        CIN_UNITS = [128, 128, 128]
        BATCH = 1024
        key = jax.random.key(seed)
        ks = jax.random.split(key, 9)
        inputs = jax.random.normal(ks[0], (BATCH, NUM_FIELDS * EMBED_DIM), dtype=jnp.float32)
        W1 = jax.random.normal(ks[1], (CIN_UNITS[0], NUM_FIELDS * NUM_FIELDS), dtype=jnp.float32) * 0.02
        b1 = jax.random.normal(ks[2], (CIN_UNITS[0],), dtype=jnp.float32) * 0.02
        W2 = jax.random.normal(ks[3], (CIN_UNITS[1], NUM_FIELDS * CIN_UNITS[0]), dtype=jnp.float32) * 0.02
        b2 = jax.random.normal(ks[4], (CIN_UNITS[1],), dtype=jnp.float32) * 0.02
        W3 = jax.random.normal(ks[5], (CIN_UNITS[2], NUM_FIELDS * CIN_UNITS[1]), dtype=jnp.float32) * 0.02
        b3 = jax.random.normal(ks[6], (CIN_UNITS[2],), dtype=jnp.float32) * 0.02
        fc_W = jax.random.normal(ks[7], (1, sum(CIN_UNITS)), dtype=jnp.float32) * 0.02
        fc_b = jax.random.normal(ks[8], (1,), dtype=jnp.float32) * 0.02
        return {'inputs': inputs, 'W1': W1, 'b1': b1, 'W2': W2, 'b2': b2, 'W3': W3, 'b3': b3, 'fc_W': fc_W, 'fc_b': fc_b}
    _L0_rec_all = _L0_rec_setup()
    _L0_rec_in = {k: v for k, v in _L0_rec_all.items() if k in ('W1', 'b1', 'W2', 'b2', 'W3', 'b3', 'fc_W', 'fc_b')}
    del _L0_rec_all
    return {'r_inputs': r_inputs, 'L0_rec_W1': _L0_rec_in['W1'], 'L0_rec_b1': _L0_rec_in['b1'], 'L0_rec_W2': _L0_rec_in['W2'], 'L0_rec_b2': _L0_rec_in['b2'], 'L0_rec_W3': _L0_rec_in['W3'], 'L0_rec_b3': _L0_rec_in['b3'], 'L0_rec_fc_W': _L0_rec_in['fc_W'], 'L0_rec_fc_b': _L0_rec_in['fc_b']}

def reference(r_inputs, L0_rec_W1, L0_rec_b1, L0_rec_W2, L0_rec_b2, L0_rec_W3, L0_rec_b3, L0_rec_fc_W, L0_rec_fc_b):
    import jax
    import jax.numpy as jnp

    def _L0_rec_ref(inputs, W1, b1, W2, b2, W3, b3, fc_W, fc_b):
        import jax, jax.numpy as jnp
        import numpy as np
        NUM_FIELDS = 32
        EMBED_DIM = 64
        CIN_UNITS = [128, 128, 128]
        BATCH = 1024
        X0 = inputs.reshape(-1, NUM_FIELDS, EMBED_DIM)
        Xi = X0
        pools = []
        for W, b in ((W1, b1), (W2, b2), (W3, b3)):
            out_ch = W.shape[0]
            m = Xi.shape[1]
            Wr = W.reshape(out_ch, NUM_FIELDS, m)
            Xi = jnp.einsum('bhd,bmd,ohm->bod', X0, Xi, Wr) + b[None, :, None]
            pools.append(Xi.sum(axis=-1))
        concat = jnp.concatenate(pools, axis=-1)
        return concat @ fc_W.T + fc_b
    y = _L0_rec_ref(r_inputs, L0_rec_W1, L0_rec_b1, L0_rec_W2, L0_rec_b2, L0_rec_W3, L0_rec_b3, L0_rec_fc_W, L0_rec_fc_b)
    return y

_drawn_inputs = setup_inputs


def setup_inputs(seed=0):
    import zlib

    import numpy as np

    out = dict(_drawn_inputs(seed))
    spreads = {}
    factors = {}
    for name, (base, spread) in spreads.items():
        noise = np.random.default_rng([zlib.crc32(name.encode()), seed]).standard_normal(out[name].shape)
        drawn = base * np.exp(spread * noise) if base else spread * noise
        out[name] = jnp.asarray(drawn.astype(out[name].dtype))
    for name, factor in factors.items():
        out[name] = (out[name] * factor).astype(out[name].dtype)
    return out
```

```python
from contextlib import ExitStack

import concourse.bass as bass
from concourse import mybir

P = 128
B = 64
H = 32
D = 64
M = 128
COLS = B * D
N = 512
CHUNKS = COLS // N
J = P // H
TILES = 4
DVE_TILES = 3
HALF = H // 2

FIRST = [0, 0, 3, 2]
STEP = [0, 4, 8, 4]
PAIR = [(0, 1), (1, 2), (3, 2), (0, 3)]
TURNED = FIRST[2] + STEP[2] * (J - 1) + H
ROWS = TILES * P + 3 * HALF
PART_ROWS = 15
PARTS = [(0, 15), (15, 30), (30, H)]
V_PARTS = 4
V_POOL = (1, 3)


def cin_kernel(nc, x2, w1, w2, w3, vecs, fc3, fc_b, out):
    f32 = mybir.dt.float32
    f32r = mybir.dt.float32r
    ALU = mybir.AluOpType
    ACT = mybir.ActivationFunctionType
    AX = mybir.AxisListType

    ctx = ExitStack()
    with ctx:
        def sb(name, shape, dt=f32):
            return ctx.enter_context(nc.sbuf_tensor(name, shape, dt))

        def pb(name, shape):
            return ctx.enter_context(nc.psum_tensor(name, shape, f32))

        def sem(name):
            return ctx.enter_context(nc.semaphore(name))

        early = ExitStack()
        half_feat = CHUNKS // 2 * 2 * TILES * N
        taken = [0]

        def early_sb(name, shape, dt=f32):
            size = 1
            for extent in shape[1:]:
                size *= extent
            taken[0] += (size + 7) // 8 * 8
            return early.enter_context(nc.sbuf_tensor(name, shape, dt))

        early_sb("features_of_chunks_0_to_3", [P, half_feat])
        w3_sb = early_sb("w3_sb", [P, H, M])
        w1_sb = early_sb("w1_sb", [P, 2, ROWS])
        xp = early_sb("xp", [P, D // 4, B])
        fc3_all = early_sb("fc3_all", [P, M])
        v_rep = early_sb("v_rep", [P, H, 4])
        xp_hi = early_sb("xp_hi", [P, D // 4 * B], f32r)
        xp_lo = early_sb("xp_lo", [P, D // 4 * B], f32r)
        w2_sb = early_sb("w2_sb", [P, H * M])
        a_sb = early_sb("a_sb", [P, TURNED, H + 1])
        v_all = early_sb("v_all", [P, H, H + 1])
        rows_sb = early_sb("rows_sb", [P, ROWS + 3 * H])
        assert taken[0] <= 2 * half_feat
        early_sb("x1_of_chunks_0_to_3", [P, 2 * half_feat - taken[0] + CHUNKS // 2 * N])
        xa16 = early_sb("xa16", [P, N])
        xb16 = early_sb("xb16", [P, N])
        z16_hi = early_sb("z16_hi", [P, N], f32r)
        z16_lo = early_sb("z16_lo", [P, N], f32r)
        early.close()
        feat = sb("feat", [P, CHUNKS, 2, TILES, N], f32r)
        x1 = sb("x1", [P, CHUNKS, N])

        tail = sb("tail", [3 * HALF, CHUNKS, N], f32r)
        lin = sb("lin", [3 * H, CHUNKS, N], f32r)
        rep = sb("rep", [P, 2, 4, N])
        z_pool = sb("z_pool", [P, 2, N])
        w1_hi = sb("w1_hi", [P, TILES, M], f32r)
        w1_lo = sb("w1_lo", [P, TILES, M], f32r)
        w1_tail = sb("w1_tail", [3 * HALF, M], f32r)
        a_hi = sb("a_hi", [P, TILES, M], f32r)
        a_lo = sb("a_lo", [P, TILES, M], f32r)
        a_tail = sb("a_tail", [3 * HALF, M], f32r)
        c_w = sb("c_w", [3 * H, M], f32r)
        ident = sb("ident", [P, P])
        vec = sb("vec", [P, 6])
        b23 = sb("b23", [P, 2])
        v2 = sb("v2", [P, 2, H])
        q_sb = sb("q_sb", [P, 1])
        ones = sb("ones", [P, 1])
        xsum = sb("xsum", [P, B])
        total = sb("total", [P, 2, B])
        y_sb = sb("y_sb", [1, B])
        fcb_sb = sb("fcb_sb", [1, 1])

        z_ps = pb("z_ps", [P, DVE_TILES, N])
        x1_ps = [pb("x1_ps0", [P, N]), pb("x1_ps1", [P, N])]
        a_ps = [pb("a_ps0", [P, N]), pb("a_ps1", [P, N])]
        misc_ps = pb("misc_ps", [P, N])
        part_ps = [a_ps[0], a_ps[1], misc_ps]
        q_ps = misc_ps[:, 500:501]
        y_ps = misc_ps[0:1, 0:B]

        rep_in = [[sem(f"rep_in{i}_{r}") for r in range(4)] for i in range(2)]
        vec_in, w1_in, x16_in, xp_in = sem("vec_in"), sem("w1_in"), sem("x16_in"), sem("xp_in")
        w3_in = [sem(f"w3_in{i}") for i in range(V_PARTS)]
        w2_in = [sem("w2_in0"), sem("w2_in1")]
        tail_in, lin_lo_in, out_done = sem("tail_in"), sem("lin_lo_in"), sem("out_done")
        z_done, zp_done, hi_done, lo_done = sem("z_done"), sem("zp_done"), sem("hi_done"), sem("lo_done")
        z16_done, hi16_done, lo16_done = sem("z16_done"), sem("hi16_done"), sem("lo16_done")
        xp_hi_done, xp_lo_done, lin_hi_done = sem("xp_hi_done"), sem("xp_lo_done"), sem("lin_hi_done")
        ident_done, ones_done, b23_done = sem("ident_done"), sem("ones_done"), sem("b23_done")
        w1_rows, a_rows = sem("w1_rows"), sem("a_rows")
        wt_ready, wt_hi, wt_lo = sem("wt_ready"), sem("wt_hi"), sem("wt_lo")
        v_terms, v_terms_pool, v_ready, v_saved = sem("v_terms"), sem("v_terms_pool"), sem("v_ready"), sem("v_saved")
        a_ready, a_saved = sem("a_ready"), sem("a_saved")
        q_ready, q_saved = sem("q_ready"), sem("q_saved")
        x1_ready, x1_saved = sem("x1_ready"), sem("x1_saved")
        b_ready, prod_done, xsum_done = sem("b_ready"), sem("prod_done"), sem("xsum_done")
        acc_done, total_done, y_ready, y_done = sem("acc_done"), sem("total_done"), sem("y_ready"), sem("y_done")
        FIRST_BETWEEN = 5
        W1_ROWS, A_ROWS = 2, 7

        def strided(view, offset, dims):
            return bass.AP(view.tensor, offset, [list(view.ap[0])] + dims)

        def products_done(engine, c, k):
            if k < DVE_TILES:
                engine.wait_ge(z_done, DVE_TILES * c + k + 1)
            else:
                engine.wait_ge(zp_done, c + 1)

        def product_of(c, k):
            return z_ps[:, k, :] if k < DVE_TILES else z_pool[:, c % 2, :]

        def terms_of_v(engine, maker, i, done):
            hs = slice(i * H // V_PARTS, (i + 1) * H // V_PARTS)
            engine.wait_ge(vec_in, 48)
            engine.wait_ge(w3_in[i], 16)
            fc = fc3_all[:, :].rearrange("q (r p) -> q r p", r=1).to_broadcast([P, H // V_PARTS, M])
            maker.tensor_tensor(w3_sb[:, hs, :], w3_sb[:, hs, :], fc, ALU.mult).then_inc(done, 1)

        def features_free(engine, c):
            if c == CHUNKS // 2:
                engine.wait_ge(v_ready, V_PARTS)
            if c == CHUNKS // 2 + 1:
                engine.wait_ge(w1_rows, W1_ROWS)
                engine.wait_ge(q_ready, 1)
                engine.wait_ge(xp_lo_done, 1)
                engine.wait_ge(xsum_done, 4)
                engine.wait_ge(lin_lo_in, 16)
            if c == CHUNKS // 2 + 2:
                engine.wait_ge(a_ready, len(PARTS))
            if c == CHUNKS // 2 + 3:
                engine.wait_ge(a_rows, A_ROWS)
                engine.wait_ge(wt_ready, 2)

        block = ctx.enter_context(nc.Block())

        @block.sync
        def _(sp):
            def load_replicas(c):
                for r in range(4):
                    if c >= 2:
                        last_tile = (0, 1, 2, 2)[r]
                        sp.wait_ge(z_done, DVE_TILES * (c - 2) + last_tile + 1)
                        if r == 0:
                            sp.wait_ge(lin_hi_done, c - 1)
                        if r in PAIR[DVE_TILES]:
                            sp.wait_ge(zp_done, c - 1)
                    src = bass.AP(x2.tensor, FIRST[r] * COLS + c * N,
                                  [[STEP[r] * COLS, J], [COLS, H], [1, N]])
                    sp.dma_start(rep[:, c % 2, r, :], src).then_inc(rep_in[c % 2][r], 16)

            half_w = H * M // 2
            sp.dma_start(w1_sb[:, :, :], w1).then_inc(w1_in, 16)
            load_replicas(0)
            sp.dma_start(vec[:, :], vecs).then_inc(vec_in, 16)
            sp.dma_start(fcb_sb[:, :], fc_b).then_inc(vec_in, 16)
            sp.dma_start(fc3_all[:, :], fc3.partition_broadcast(P)).then_inc(vec_in, 16)
            sp.dma_start(xa16[:, :], x2[0:HALF, :].rearrange("h (c n) -> (h c) n", n=N)).then_inc(x16_in, 16)
            sp.dma_start(xb16[:, :], x2[HALF:H, :].rearrange("h (c n) -> (h c) n", n=N)).then_inc(x16_in, 16)
            for i in range(V_PARTS):
                hs = slice(i * H // V_PARTS, (i + 1) * H // V_PARTS)
                sp.dma_start(w3_sb[:, hs, :], w3[:, hs, :]).then_inc(w3_in[i], 16)
            load_replicas(1)
            sp.dma_start(w2_sb[:, 0:half_w], w2[:, 0:half_w]).then_inc(w2_in[0], 16)
            sp.dma_start(w2_sb[:, half_w:], w2[:, half_w:]).then_inc(w2_in[1], 16)
            for row, part, done in ((0, z16_hi, hi16_done), (2, z16_hi, hi16_done), (1, z16_lo, lo16_done)):
                sp.wait_ge(done, 1)
                sp.dma_start(tail[row * HALF:(row + 1) * HALF, :, :].bitcast(f32),
                             part[:, :].bitcast(f32)).then_inc(tail_in, 16)
            sp.dma_start(xp[:, :, :].rearrange("p d b -> p (d b)"),
                         x2[0:H, :].rearrange("h (c n) -> (h c) n", c=4)).then_inc(xp_in, 16)
            load_replicas(2)
            load_replicas(3)
            sp.wait_ge(xp_lo_done, 1)
            sp.dma_start(lin[2 * H:3 * H, :, :].rearrange("h c n -> h (c n)").bitcast(f32),
                         xp_lo[:, :].bitcast(f32)).then_inc(lin_lo_in, 16)
            for c in range(4, CHUNKS):
                load_replicas(c)
            sp.wait_ge(y_done, 1)
            sp.dma_start(out, y_sb[:, :]).then_inc(out_done, 16)
            sp.wait_ge(out_done, 16)

        @block.gpsimd
        def _(pool):
            def pairs(c):
                left, right = PAIR[DVE_TILES]
                for r in (left, right):
                    pool.wait_ge(rep_in[c % 2][r], 16 * (c // 2 + 1))
                if c >= 2:
                    pool.wait_ge(hi_done, TILES * (c - 1))
                    pool.wait_ge(lo_done, TILES * (c - 1))
                nc.gpsimd.tensor_tensor(z_pool[:, c % 2, :], rep[:, c % 2, left, :], rep[:, c % 2, right, :],
                                        ALU.mult).then_inc(zp_done, 1)

            def split16():
                pool.wait_ge(x16_in, 32)
                nc.gpsimd.tensor_tensor(xa16[:, :], xa16[:, :], xb16[:, :], ALU.mult).then_inc(z16_done, 1)
                pool.wait_ge(z16_done, 1)
                pool.wait_ge(hi16_done, 1)
                nc.gpsimd.tensor_tensor(z16_lo[:, :], xa16[:, :], z16_hi[:, :].bitcast(f32),
                                        ALU.subtract).then_inc(lo16_done, 1)

            def split_x():
                pool.wait_ge(xp_in, 16)
                pool.wait_ge(xp_hi_done, 1)
                nc.gpsimd.tensor_tensor(xp_lo[:, :], xp[:, :, :].rearrange("p d b -> p (d b)"),
                                        xp_hi[:, :].bitcast(f32), ALU.subtract).then_inc(xp_lo_done, 1)

            def sum_x():
                pool.wait_ge(xp_lo_done, 1)
                left, steps = D // 8, 0
                while left:
                    if steps:
                        pool.wait_ge(xsum_done, steps)
                    dst = xp[:, 0:left, :] if left > 1 else xsum[:, :].rearrange("p (n b) -> p n b", n=1)
                    nc.gpsimd.tensor_tensor(dst, xp[:, 0:left, :], xp[:, left:2 * left, :],
                                            ALU.add).then_inc(xsum_done, 1)
                    left, steps = left // 2, steps + 1

            def gather(c):
                pool.wait_ge(prod_done, c + 1)
                if c > 1:
                    pool.wait_ge(acc_done, c - 1)
                nc.gpsimd.tensor_tensor(x1[:, 0, :], x1[:, 0, :], x1[:, c, :], ALU.add).then_inc(acc_done, 1)

            nc.gpsimd.memset(ident[:, :], 0.0).then_inc(ident_done, 1)
            nc.gpsimd.memset(ones[:, :], 1.0).then_inc(ones_done, 1)
            pool.wait_ge(ident_done, 1)
            nc.gpsimd.affine_select(out=ident[:, :], in_=ident[:, :], compare_op=ALU.not_equal, fill=1.0,
                                    base=0, pattern=[[-1, P]], channel_multiplier=1).then_inc(ident_done, 1)
            pairs(0)
            for i in V_POOL:
                terms_of_v(pool, nc.gpsimd, i, v_terms_pool)
            pairs(1)
            split16()
            pool.wait_ge(vec_in, 48)
            nc.gpsimd.tensor_scalar(b23[:, :], vec[:, 1:3], float(D), 0.0, ALU.mult, ALU.add).then_inc(b23_done, 1)
            split_x()
            pairs(2)
            sum_x()
            for c in range(3, CHUNKS):
                pairs(c)
                if c >= 5:
                    gather(c - 4)
            for c in range(CHUNKS - 4, CHUNKS - 1):
                gather(c)

        @block.scalar
        def _(act):
            def copy(dst, src):
                return nc.scalar.activation(dst, src, ACT.Copy)

            def hi(n):
                c, k = divmod(n, TILES)
                if k == 0:
                    features_free(act, c)
                products_done(act, c, k)
                copy(feat[:, c, 0, k, :], product_of(c, k)).then_inc(hi_done, 1)

            def lin_hi(c):
                act.wait_ge(rep_in[c % 2][0], 16 * (c // 2 + 1))
                copy(lin[0:2 * H, c, :], rep[0:2 * H, c % 2, 0, :]).then_inc(lin_hi_done, 1)

            def save_x1(c):
                if c == 0:
                    act.wait_ge(vec_in, 48)
                if c == CHUNKS // 2:
                    act.wait_ge(lo16_done, 1)
                    act.wait_ge(tail_in, 48)
                act.wait_ge(x1_ready, max(c + 1, 2))
                nc.scalar.activation(x1[:, c, :], x1_ps[c % 2][:, :], ACT.Identity,
                                     bias=vec[:, 0:1]).then_inc(x1_saved, 1)

            def weights_hi(n):
                main, tl = (w1_hi, w1_tail) if n == 0 else (a_hi, a_tail)
                act.wait_ge(wt_ready, n + 1)
                copy(main[:, :, :], a_ps[0][:, :].rearrange("p (k m) -> p k m", m=M)).then_inc(wt_hi, 1)
                copy(tl[:, :], a_ps[1][0:3 * HALF, 0:M]).then_inc(wt_hi, 1)
                if n == 1:
                    copy(c_w[:, :], a_ps[1][0:3 * H, M:2 * M]).then_inc(wt_hi, 1)

            def save_fc2():
                act.wait_ge(vec_in, 48)
                copy(v_all[:, :, H:H + 1], vec[:, 4:5].rearrange("p (h r) -> p h r", r=1).to_broadcast(
                    [P, H, 1])).then_inc(v_saved, 1)

            def save_v():
                act.wait_ge(v_ready, V_PARTS)
                copy(v2[:, 1, :], v2[:, 0, :]).then_inc(v_saved, 1)
                act.wait_ge(v_saved, 2)
                copy(v_all[:, :, 0:H], strided(v2[:, :, :], 0, [[1, H], [1, H]])).then_inc(v_saved, 1)
                copy(v_rep[:, :, :], strided(v2[:, :, :], 0, [[1, H], [0, 4]])).then_inc(v_saved, 1)

            def save_q():
                act.wait_ge(q_ready, 1)
                copy(q_sb[:, :], q_ps).then_inc(q_saved, 1)

            def save_a(i):
                a0, a1 = PARTS[i]
                act.wait_ge(a_ready, i + 1)
                src = part_ps[i][:, 0:(a1 - a0) * (H + 1)].rearrange("p (a s) -> p a s", s=H + 1)
                copy(a_sb[:, a0:a1, :], src).then_inc(a_saved, 1)
                again = min(a1, TURNED - H) - a0
                if again > 0:
                    copy(a_sb[:, H + a0:H + a0 + again, :], src[:, 0:again, :]).then_inc(a_saved, 1)

            def hi16():
                act.wait_ge(z16_done, 1)
                copy(z16_hi[:, :], xa16[:, :]).then_inc(hi16_done, 1)

            def xp_split():
                act.wait_ge(xp_in, 16)
                copy(xp_hi[:, :], xp[:, :, :].rearrange("p d b -> p (d b)")).then_inc(xp_hi_done, 1)

            extra = {0: [lambda: weights_hi(0)], 3: [lambda: lin_hi(0), save_fc2, save_v], 5: [hi16],
                     7: [lambda: lin_hi(1), save_q, xp_split, lambda: save_a(0),
                         lambda: save_x1(0), lambda: save_x1(1)],
                     8: [lambda: lin_hi(2)], 10: [lambda: save_a(1)], 11: [lambda: save_a(2)],
                     12: [lambda: weights_hi(1)], 14: [lambda: save_x1(2)]}
            for c in range(3, CHUNKS):
                extra.setdefault(TILES * c + (1 if c == 3 else 0), []).append(lambda c=c: lin_hi(c))
                extra.setdefault(22 + 5 * (c - 3), []).append(lambda c=c: save_x1(c))
            for n in range(TILES * CHUNKS):
                hi(n)
                for f in extra.pop(n, []):
                    f()
            for n in sorted(extra):
                for f in extra[n]:
                    f()

        @block.vector
        def _(dve):
            def pairs(n):
                c, k = divmod(n, DVE_TILES)
                left, right = PAIR[k]
                for r in (left, right):
                    dve.wait_ge(rep_in[c % 2][r], 16 * (c // 2 + 1))
                if c >= 1:
                    dve.wait_ge(hi_done, TILES * (c - 1) + k + 1)
                    dve.wait_ge(lo_done, TILES * (c - 1) + k + 1)
                nc.vector.tensor_tensor(z_ps[:, k, :], rep[:, c % 2, left, :], rep[:, c % 2, right, :],
                                        ALU.mult).then_inc(z_done, 1)

            def lo(n):
                c, k = divmod(n, TILES)
                if k == 0:
                    features_free(dve, c)
                products_done(dve, c, k)
                dve.wait_ge(hi_done, n + 1)
                nc.vector.tensor_tensor(feat[:, c, 1, k, :], product_of(c, k), feat[:, c, 0, k, :].bitcast(f32),
                                        ALU.subtract).then_inc(lo_done, 1)

            def rows_of_w1():
                dve.wait_ge(w1_in, 16)
                nc.vector.tensor_tensor(rows_sb[:, H:ROWS], w1_sb[:, 0, H:], w1_sb[:, 1, H:],
                                        ALU.add).then_inc(w1_rows, 1)
                nc.vector.tensor_copy(rows_sb[:, 0:H], w1_sb[:, 0, 0:H]).then_inc(w1_rows, 1)

            def rows_of_a():
                dve.wait_ge(a_saved, 5)
                dve.wait_ge(wt_ready, 1)
                wide = H + 1

                def both(dst, start, shift, outer, inner):
                    (turn, more, times), count = outer, inner
                    first = strided(a_sb[:, :, :], start * wide + shift,
                                    [[turn * wide + more, times], [wide, count]])
                    second = strided(a_sb[:, :, :], (start + shift) * wide + H - shift,
                                     [[(turn + more) * wide - more, times], [wide, count]])
                    nc.vector.tensor_tensor(dst.rearrange("p (j h) -> p j h", h=count), first, second,
                                            ALU.add).then_inc(a_rows, 1)

                for k, (left, right) in enumerate(PAIR):
                    lead, grow = FIRST[right] - FIRST[left], STEP[right] - STEP[left]
                    j0 = 1 if k == 0 else 0
                    both(rows_sb[:, k * P + j0 * H:(k + 1) * P], FIRST[left] + STEP[left] * j0, lead + grow * j0,
                         (STEP[left], grow, J - j0), H)
                both(rows_sb[:, TILES * P:ROWS], 0, HALF, (0, 0, 3), HALF)
                nc.vector.tensor_copy(rows_sb[:, 0:H], strided(a_sb[:, :, :], 0, [[wide, H]])).then_inc(a_rows, 1)
                nc.vector.tensor_copy(rows_sb[:, ROWS:].rearrange("p (r h) -> p r h", h=H),
                                      strided(a_sb[:, :, :], H, [[0, 3], [wide, H]])).then_inc(a_rows, 1)

            def weights_lo(n):
                main, main_lo, tl = (w1_hi, w1_lo, w1_tail) if n == 0 else (a_hi, a_lo, a_tail)
                dve.wait_ge(wt_hi, 2 if n == 0 else 5)
                nc.vector.tensor_tensor(main_lo[:, :, :], a_ps[0][:, :].rearrange("p (k m) -> p k m", m=M),
                                        main[:, :, :].bitcast(f32), ALU.subtract).then_inc(wt_lo, 1)
                rows = slice(2 * HALF, 3 * HALF)
                nc.vector.tensor_tensor(tl[rows, :], a_ps[1][rows, 0:M], tl[rows, :].bitcast(f32),
                                        ALU.subtract).then_inc(wt_lo, 1)
                if n == 1:
                    rows = slice(H, 2 * H)
                    nc.vector.tensor_tensor(c_w[rows, :], a_ps[1][rows, M:2 * M], c_w[rows, :].bitcast(f32),
                                            ALU.subtract).then_inc(wt_lo, 1)

            def product(c):
                dve.wait_ge(x1_saved, c + 1)
                dve.wait_ge(b_ready, c + 1)
                nc.vector.scalar_tensor_tensor(out=x1[:, c, :], in0=a_ps[c % 2][:, :], scalar=vec[:, 3:4],
                                               in1=x1[:, c, :], op0=ALU.add, op1=ALU.mult).then_inc(prod_done, 1)

            def reduce_v(i):
                hs = slice(i * H // V_PARTS, (i + 1) * H // V_PARTS)
                if i in V_POOL:
                    dve.wait_ge(v_terms_pool, V_POOL.index(i) + 1)
                else:
                    dve.wait_ge(v_terms, len([o for o in range(i + 1) if o not in V_POOL]))
                nc.vector.tensor_reduce(v2[:, 0, hs], w3_sb[:, hs, :], axis=AX.X, op=ALU.add).then_inc(v_ready, 1)

            def make_v():
                for i in range(V_PARTS):
                    if i not in V_POOL:
                        terms_of_v(dve, nc.vector, i, v_terms)
                        if i:
                            reduce_v(i - 1)
                        reduce_v(i)
                reduce_v(V_PARTS - 1)

            extra = {0: [lambda: weights_lo(0)], 3: [make_v], 11: [rows_of_a], 12: [lambda: weights_lo(1)]}
            for c, n in enumerate((17, 19, 22, 27, 31, 32, 33, 34)):
                extra.setdefault(n, []).append(lambda c=c: product(c))
            rows_of_w1()
            ahead = 0
            for n in range(TILES * CHUNKS):
                c, k = divmod(n, TILES)
                while ahead < min(DVE_TILES * (CHUNKS if c >= 3 else c + 1), DVE_TILES * c + min(k + 3, 5)):
                    pairs(ahead)
                    ahead += 1
                lo(n)
                for f in extra.pop(n, []):
                    f()
            for n in sorted(extra):
                for f in extra[n]:
                    f()
            dve.wait_ge(acc_done, CHUNKS - 2)
            nc.vector.tensor_reduce(total[:, 0, :], x1[:, 0, :].rearrange("p (d b) -> p b d", b=B),
                                    axis=AX.X, op=ALU.add).then_inc(total_done, 1)
            dve.wait_ge(prod_done, CHUNKS)
            nc.vector.tensor_reduce(total[:, 1, :], x1[:, CHUNKS - 1, :].rearrange("p (d b) -> p b d", b=B),
                                    axis=AX.X, op=ALU.add).then_inc(total_done, 1)
            dve.wait_ge(y_ready, 1)
            nc.vector.tensor_scalar(y_sb[:, :], y_ps, fcb_sb[:, 0:1], 0.0, ALU.add, ALU.add).then_inc(y_done, 1)

        @block.tensor
        def _(pe):
            def transposes(n):
                if n == 0:
                    pe.wait_ge(ident_done, 2)
                    pe.wait_ge(w1_rows, W1_ROWS)
                else:
                    pe.wait_ge(a_rows, A_ROWS)
                    pe.wait_ge(a_saved, 5)
                for k in range(TILES):
                    nc.tensor.transpose(a_ps[0][:, k * M:(k + 1) * M], rows_sb[:, k * P:(k + 1) * P], ident[:, :])
                last = nc.tensor.transpose(a_ps[1][0:3 * HALF, 0:M], rows_sb[:, TILES * P:ROWS], ident[:, :])
                if n == 1:
                    last = nc.tensor.transpose(a_ps[1][0:3 * H, M:2 * M], rows_sb[:, ROWS:], ident[:, :])
                last.then_inc(wt_ready, 1)

            def terms(bank, c, w_hi, w_lo, w_tail, linear, between=()):
                between = list(between)
                placed = [0]

                def mm(w, f, **kw):
                    last = nc.tensor.matmul(bank, w, f, **kw)
                    placed[0] += 1
                    for _ in range(2):
                        if between and placed[0] > FIRST_BETWEEN:
                            between.pop(0)()
                    return last

                for k in range(TILES):
                    pe.wait_ge(hi_done, TILES * c + k + 1)
                    mm(w_hi[:, k, :], feat[:, c, 0, k, :], start=(k == 0), stop=False)
                    if k == 0 and c == 0:
                        pe.wait_ge(wt_lo, 5 if linear else 2)
                    mm(w_lo[:, k, :], feat[:, c, 0, k, :], start=False, stop=False)
                    pe.wait_ge(lo_done, TILES * c + k + 1)
                    mm(w_hi[:, k, :], feat[:, c, 1, k, :], start=False, stop=False)
                if linear:
                    mm(c_w[:, :], lin[:, c, :], start=False, stop=False)
                elif c == 0:
                    return None
                elif c == 1:
                    pe.wait_ge(tail_in, 48)
                return mm(w_tail[:, :], tail[:, c, :], start=False, stop=True)

            def x1_product(c, between=()):
                if c == 0:
                    pe.wait_ge(wt_hi, 2)
                if c >= 2:
                    pe.wait_ge(x1_saved, c - 1)
                last = terms(x1_ps[c % 2][:, :], c, w1_hi, w1_lo, w1_tail, False, between)
                if c:
                    last.then_inc(x1_ready, 1)

            def x1_tail_of_chunk_0():
                pe.wait_ge(tail_in, 48)
                nc.tensor.matmul(x1_ps[0][:, :], w1_tail[:, :], tail[:, 0, :],
                                 start=False, stop=True).then_inc(x1_ready, 1)

            def a_product(c):
                if c == 0:
                    pe.wait_ge(wt_hi, 5)
                    pe.wait_ge(wt_lo, 5)
                    pe.wait_ge(lin_lo_in, 16)
                if c >= 2:
                    pe.wait_ge(prod_done, c - 1)
                pe.wait_ge(lin_hi_done, c + 1)
                terms(a_ps[c % 2][:, :], c, a_hi, a_lo, a_tail, True).then_inc(b_ready, 1)

            def q_product():
                pe.wait_ge(v_saved, 4)
                nc.tensor.matmul(q_ps, v_rep[:, :, :].rearrange("p h r -> p (h r)"), vec[:, 1:2],
                                 start=True, stop=True).then_inc(q_ready, 1)

            def weight_product(a):
                if a == 0:
                    pe.wait_ge(wt_lo, 2)
                if a % (H // 2) == 0:
                    pe.wait_ge(w2_in[a // (H // 2)], 16)
                i = a // PART_ROWS
                if i == 2 and a == PARTS[i][0]:
                    pe.wait_ge(q_saved, 1)
                at = (a - PARTS[i][0]) * (H + 1)
                mm = nc.tensor.matmul(part_ps[i][:, at:at + H + 1], w2_sb[:, a * M:(a + 1) * M],
                                      v_all[:, a, :], start=True, stop=True)
                if a == PARTS[i][1] - 1:
                    mm.then_inc(a_ready, 1)

            transposes(0)
            pe.wait_ge(vec_in, 48)
            x1_product(0)
            q_product()
            x1_product(1, [lambda a=a: weight_product(a) for a in range(H // 2)])
            x1_tail_of_chunk_0()
            for a in range(H // 2, H):
                weight_product(a)
            transposes(1)
            x1_product(2)
            for c in range(CHUNKS):
                if c >= 3:
                    x1_product(c)
                a_product(c)
                if c == CHUNKS - 2:
                    pe.wait_ge(b23_done, 1)
                    pe.wait_ge(xsum_done, 4)
                    for i in range(2):
                        fc = strided(vec[:, :], 4 + i, [[0, B]])
                        nc.tensor.matmul(y_ps, b23[:, i:i + 1], fc, start=(i == 0), stop=False)
                    nc.tensor.matmul(y_ps, q_sb[:, :], xsum[:, :], start=False, stop=False)
            pe.wait_ge(ones_done, 1)
            for i in range(2):
                pe.wait_ge(total_done, i + 1)
                last = nc.tensor.matmul(y_ps, ones[:, :], total[:, i, :], start=False, stop=(i == 1))
            last.then_inc(y_ready, 1)


def pair_order():
    left, right = [], []
    for l, r in PAIR:
        for j in range(J):
            left += [(FIRST[l] + STEP[l] * j + h) % H for h in range(H)]
            right += [(FIRST[r] + STEP[r] * j + h) % H for h in range(H)]
    for _ in range(3):
        left += range(HALF)
        right += range(HALF, H)
    return left, right


def kernel(**inputs):
    import numpy as np
    import concourse.bacc as bacc
    from concourse import mybir as _mybir
    from concourse.bass_utils import run_bass_kernel_spmd

    x = np.ascontiguousarray(inputs["r_inputs"]).reshape(B, H, D).transpose(1, 2, 0).reshape(H, COLS)
    w1 = np.asarray(inputs["L0_rec_W1"]).reshape(M, H, H)
    left, right = pair_order()
    vectors = [inputs["L0_rec_b1"], inputs["L0_rec_b2"], inputs["L0_rec_b3"]]
    vectors += list(np.asarray(inputs["L0_rec_fc_W"]).reshape(3, M))
    arrays = {
        "x2": np.ascontiguousarray(np.concatenate([x, x], axis=0)),
        "w1": np.ascontiguousarray(np.stack([w1[:, left, right], w1[:, right, left]], axis=1)),
        "w2": np.ascontiguousarray(inputs["L0_rec_W2"]),
        "w3": np.ascontiguousarray(np.asarray(inputs["L0_rec_W3"]).reshape(M, H, M).transpose(2, 1, 0)),
        "vecs": np.ascontiguousarray(np.stack([np.asarray(v) for v in vectors], axis=1)),
        "fc3": np.ascontiguousarray(vectors[5]),
        "fc_b": np.ascontiguousarray(np.asarray(inputs["L0_rec_fc_b"]).reshape(1, 1)),
    }
    nc = bacc.Bacc("TRN2", target_bir_lowering=False, num_devices=1)
    args = [nc.dram_tensor(n, a.shape, _mybir.dt.from_np(a.dtype), kind="ExternalInput").ap()
            for n, a in arrays.items()]
    args.append(nc.dram_tensor("y", (1, B), _mybir.dt.float32, kind="ExternalOutput").ap())
    cin_kernel(nc, *args)
    r = run_bass_kernel_spmd(nc, [arrays], core_ids=[0])
    return r.results[0]["y"].reshape(B, 1)
```
